# Optimizing a Trainium2 kernel written in Bass

```python
import numpy as np
import jax
import jax.numpy as jnp

def _softmax(x, axis=-1):
    return jax.nn.softmax(x, axis=axis)

def _gelu(x):
    return jax.nn.gelu(x, approximate=True)

def _silu(x):
    return jax.nn.silu(x)

def _sigmoid(x):
    return jax.nn.sigmoid(x)

def _layernorm(x, axis=-1, eps=1e-05):
    m = jnp.mean(x, axis=axis, keepdims=True)
    v = jnp.var(x, axis=axis, keepdims=True)
    return (x - m) / jnp.sqrt(v + eps)

def _scatter_add(tgt, idx, src, axis=0):
    return tgt.at[idx].add(src)

def _segment_sum(src, seg, n):
    return jax.ops.segment_sum(src, seg, n)
kernel_name = 'mk_gnn_preln_d1_gnn_r8_2a7d73'

def setup_inputs(seed: int=0):
    np.random.seed(seed)
    _w = jnp.asarray

    def _rec_inputs():
        import jax
        import jax.numpy as jnp
        _gk = jax.random.key(seed)
        x = -0.0001006 + 1 * jax.random.normal(jax.random.fold_in(_gk, 1), (12500, 96), jnp.float32)
        src = jax.random.randint(jax.random.fold_in(_gk, 2), (400000,), 0, 12500, jnp.int32)
        dst = jnp.minimum((12500 * jax.random.uniform(jax.random.fold_in(_gk, 3), (400000,)) ** 2.0).astype(jnp.int32), 99999)
        _o = jnp.argsort(dst, stable=True)
        src = src[_o]
        dst = dst[_o]
        edge_attr_32 = 0.000196303 + 1.00016 * jax.random.normal(jax.random.fold_in(_gk, 11), (400000, 32), jnp.float32)
        return (x, src, dst, edge_attr_32)
    x, src, dst, edge_attr_32 = _rec_inputs()

    def _L0_gnn_setup():
        import jax, jax.numpy as jnp
        import numpy as np
        N, E = (6250, 100000)
        DIN = DOUT = 96
        DE = 32

        def _egnn_conv(x, src, dst, edge_attr, W_msg, W_edge, W_root, b):
            msg = x[src] @ W_msg + edge_attr @ W_edge
            agg = jax.ops.segment_max(msg, dst, num_segments=x.shape[0])
            agg = jnp.where(jnp.isneginf(agg), 0.0, agg)
            return agg + x @ W_root + b
        key = jax.random.key(seed)
        ks = jax.random.split(key, 10)
        rn = lambda k, sh, sc: jax.random.normal(k, sh, jnp.float32) * sc
        return {'X': rn(ks[0], (N, DIN), 1.0), 'edge_index': jax.random.randint(ks[1], (2, E), 0, N, jnp.int32), 'edge_attr': rn(ks[2], (E, DE), 1.0), 'W1_msg': rn(ks[3], (DIN, DOUT), DIN ** (-0.5)), 'W1_edge': rn(ks[4], (DE, DOUT), DE ** (-0.5)), 'W1_root': rn(ks[5], (DIN, DOUT), DIN ** (-0.5)), 'b1': jnp.zeros((DOUT,), jnp.float32), 'W2_msg': rn(ks[6], (DOUT, DOUT), DOUT ** (-0.5)), 'W2_edge': rn(ks[7], (DE, DOUT), DE ** (-0.5)), 'W2_root': rn(ks[8], (DOUT, DOUT), DOUT ** (-0.5)), 'b2': jnp.zeros((DOUT,), jnp.float32)}
    _L0_gnn_all = _L0_gnn_setup()
    _L0_gnn_in = {k: v for k, v in _L0_gnn_all.items() if k in ('W1_msg', 'W1_edge', 'W1_root', 'b1', 'W2_msg', 'W2_edge', 'W2_root', 'b2')}
    del _L0_gnn_all
    return {'x': x, 'src': src, 'dst': dst, 'edge_attr_32': edge_attr_32, 'L0_gnn_W1_msg': _L0_gnn_in['W1_msg'], 'L0_gnn_W1_edge': _L0_gnn_in['W1_edge'], 'L0_gnn_W1_root': _L0_gnn_in['W1_root'], 'L0_gnn_b1': _L0_gnn_in['b1'], 'L0_gnn_W2_msg': _L0_gnn_in['W2_msg'], 'L0_gnn_W2_edge': _L0_gnn_in['W2_edge'], 'L0_gnn_W2_root': _L0_gnn_in['W2_root'], 'L0_gnn_b2': _L0_gnn_in['b2']}

def reference(x, src, dst, edge_attr_32, L0_gnn_W1_msg, L0_gnn_W1_edge, L0_gnn_W1_root, L0_gnn_b1, L0_gnn_W2_msg, L0_gnn_W2_edge, L0_gnn_W2_root, L0_gnn_b2):
    import jax
    import jax.numpy as jnp

    def _L0_gnn_ref(X, edge_index, edge_attr, W1_msg, W1_edge, W1_root, b1, W2_msg, W2_edge, W2_root, b2):
        import jax, jax.numpy as jnp
        import numpy as np
        N, E = (6250, 100000)
        DIN = DOUT = 96
        DE = 32

        def _egnn_conv(x, src, dst, edge_attr, W_msg, W_edge, W_root, b):
            msg = x[src] @ W_msg + edge_attr @ W_edge
            agg = jax.ops.segment_max(msg, dst, num_segments=x.shape[0])
            agg = jnp.where(jnp.isneginf(agg), 0.0, agg)
            return agg + x @ W_root + b
        src, dst = (edge_index[0], edge_index[1])
        c1 = jax.nn.leaky_relu(_egnn_conv(X, src, dst, edge_attr, W1_msg, W1_edge, W1_root, b1))
        c2 = jax.nn.leaky_relu(_egnn_conv(c1, src, dst, edge_attr, W2_msg, W2_edge, W2_root, b2))
        return c2
    edge_index = jnp.stack([src, dst])
    h = jnp.maximum(_layernorm(x, axis=-1), 0.0)
    x = x + _L0_gnn_ref(h, edge_index, edge_attr_32, L0_gnn_W1_msg, L0_gnn_W1_edge, L0_gnn_W1_root, L0_gnn_b1, L0_gnn_W2_msg, L0_gnn_W2_edge, L0_gnn_W2_root, L0_gnn_b2)
    return x

_drawn_inputs = setup_inputs


def setup_inputs(seed=0):
    import zlib

    import numpy as np

    out = dict(_drawn_inputs(seed))
    spreads = {'L0_gnn_b1': (0.0, 0.295), 'L0_gnn_b2': (0.0, 0.429)}
    factors = {}
    for name, (base, spread) in spreads.items():
        noise = np.random.default_rng([zlib.crc32(name.encode()), seed]).standard_normal(out[name].shape)
        drawn = base * np.exp(spread * noise) if base else spread * noise
        out[name] = jnp.asarray(drawn.astype(out[name].dtype))
    for name, factor in factors.items():
        out[name] = (out[name] * factor).astype(out[name].dtype)
    return out
```

```python
from contextlib import ExitStack

import numpy as np

import concourse.bass as bass
from concourse import mybir
from concourse.alu_op_type import AluOpType as ALU

F32 = mybir.dt.float32
BF16 = mybir.dt.bfloat16
I32 = mybir.dt.int32
ACT = mybir.ActivationFunctionType
AX = mybir.AxisListType

P = 128
N, D = 12500, 96
E, DE = 400000, 32
EPS = 1e-5
SLOPE = 0.01
LOW = -3.0e38

NP = 125
NODES = N // NP
GT = 10
NG = NODES // GT
TP_BANKS = [4, 4, 2]
HALVES = 2
HT = GT // HALVES

EPP = E // P
T = 25
RING = 5
STEPS = EPP // (T * RING)
QUADS = [(4 * g, min(4, T - 4 * g)) for g in range((T + 3) // 4)]
NQ = len(QUADS)
BANKS = 5
NT = len(TP_BANKS)

SPARE = E
ZERO = E + P
ROWS = E + 2 * P


def wait_slot(engine, semaphore, count):
    if not isinstance(count, int) or count > 0:
        engine.wait_ge(semaphore, count)


def freed_columns(g):
    last = g - BANKS if g >= BANKS else g - BANKS + NQ
    return min(4 * (last + 1), T) - (0 if g >= BANKS else T)


assert NP * NODES == N and NG * GT == NODES and sum(TP_BANKS) == GT
assert P * EPP == E and STEPS * RING * T == EPP and (RING * NQ) % BANKS == 0 and T % 4 == 1


def build(nc, x, src, dst, edge_attr, w_msg, w_edge, w_root, bias, out):
    with ExitStack() as ctx:
        def sb(name, shape, dt=F32):
            return ctx.enter_context(nc.sbuf_tensor(name, shape, dt))

        def ps(name):
            return ctx.enter_context(nc.psum_tensor(name, [P, 512], F32))

        def sem(name):
            return ctx.enter_context(nc.semaphore(name))

        def sems(name, n):
            return [sem(f"{name}{i}") for i in range(n)]

        msg_table = [nc.dram_tensor(f"msg_table{l}", (N, D), F32).ap() for l in range(2)]
        root_table = [nc.dram_tensor(f"root_table{l}", (N, D), F32).ap() for l in range(2)]
        run_rows = nc.dram_tensor("run_rows", (ROWS, D), F32).ap()
        end_rows = nc.dram_tensor("end_rows", (NP, NODES), I32).ap()

        def by_group(a):
            return a.rearrange("(p q j) f -> p q (j f)", p=NP, q=NG)

        def by_chunk(a):
            return a.rearrange("(p k t) f -> p k (t f)", p=P, t=T)

        src_chunks = src.rearrange("(p k t) -> p k t", p=P, t=T)
        dst_rows = dst.rearrange("(p e) -> p e", p=P)
        attr_chunks = by_chunk(edge_attr)
        run_chunks = by_chunk(run_rows[0:E, :])
        end_groups = end_rows.rearrange("p (q j) -> p q j", q=NG)

        ident = sb("ident", [P, P])
        before = sb("before", [P, P])
        iota_i = sb("iota_i", [P, P], I32)
        iota_b = sb("iota_b", [P, P], BF16)
        part_i = sb("part_i", [P, 1], I32)
        w_node = [sb(f"w_node{l}", [D, 2 * D]) for l in range(2)]
        w_blocks = [sb(f"w_blocks{l}", [P, 4 * D]) for l in range(2)]
        bias_rep = [sb(f"bias_rep{l}", [NP, D]) for l in range(2)]
        eps = sb("eps", [P, 1])
        penalty = sb("penalty", [P, EPP])
        node_p = sb("node_p", [P, EPP], BF16)
        node_j = sb("node_j", [P, EPP], BF16)
        hot = sb("hot", [P, T * (NP + NODES) + 1], BF16)
        hot_p = hot[:, 0:T * NP].rearrange("p (t n) -> p t n", n=NP)
        hot_j = hot[:, T * NP + 1:T * (NP + NODES) + 1].rearrange("p (t n) -> p t n", n=NODES)
        rows = sb("rows", [P, RING, T * D])
        run = sb("run", [P, RING, T * D])
        attr = sb("attr", [P, RING, T * DE])
        attr_t = sb("attr_t", [P, RING, NQ * P])
        ids = sb("ids", [P, RING, T], I32)
        pen = sb("pen", [P, T])
        node_in = sb("node_in", [NP, 2, GT * D])
        root_in = sb("root_in", [NP, 2, GT * D])
        msg_out = sb("msg_out", [NP, 2, GT * D])
        root_out = sb("root_out", [NP, 2, GT * D])
        node_t = hot[0:D, 0:2 * GT * NP].bitcast(F32)
        end_ids = sb("end_ids", [NP, 2, GT], I32)
        stats = sb("stats", [NP, GT, 6])
        moments = sb("moments", [NP, GT, 2])
        std = sb("std", [NP, GT])
        rstd = sb("rstd", [NP, GT])
        hist = sb("hist", [NP, NODES])
        hist_sum = sb("hist_sum", [NP, 1])
        hist_before = sb("hist_before", [NP, 1])
        ends = sb("ends", [NP, NODES])
        some = sb("some", [NP, NODES])
        ends_i = sb("ends_i", [NP, NODES], I32)
        edge_ids = sb("edge_ids", [P, 4], I32)
        edge_f = sb("edge_f", [P, 4])
        seam = sb("seam", [P, 8])
        seam_ids = sb("seam_ids", [P, 1], I32)
        seam_pen = sb("seam_pen", [P, D])
        seam_pen_t = sb("seam_pen_t", [D, P])
        carry = sb("carry", [D, 1 + P])
        seam_rows = sb("seam_rows", [P, D])
        seam_max = sb("seam_max", [P, D])
        dst_i = run[:, 0:2, :].rearrange("p c n -> p (c n)")[:, 0:EPP].bitcast(I32)
        dst_f = run[:, 2:4, :].rearrange("p c n -> p (c n)")[:, 0:EPP]
        tmp_f = run[:, 2:5, :].rearrange("p c n -> p (c n)")[:, EPP:2 * EPP]

        bank = [ps(f"bank{i}") for i in range(BANKS)]
        turn_a, turn_b, spare_bank = ps("turn_a"), ps("turn_b"), ps("spare_bank")
        turn = [turn_a, turn_b, spare_bank]

        iotas, w_loaded, blocks_zero = sem("iotas"), sem("w_loaded"), sem("blocks_zero")
        blocks_loaded, consts_made, dst_loaded = sem("blocks_loaded"), sem("consts_made"), sem("dst_loaded")
        zero_stored, zeros_made = sem("zero_stored"), sem("zeros_made")
        waits_met = sem("waits_met")
        vec = sem("vec")
        seam_turned, ends_counted, ends_ready, ends_stored = (
            sem("seam_turned"), sem("ends_counted"), sem("ends_ready"), sem("ends_stored"))
        hot_made, hist_done, hist_added = sem("hot_made"), sem("hist_done"), sem("hist_added")

        class NodePhase:
            def __init__(s, name):
                s.name = name
                s.loaded = sems(name + "_loaded", 2)
                s.ids_loaded = sems(name + "_ids_loaded", 2)
                s.gathered = sems(name + "_gathered", 2)
                s.ready = sem(name + "_ready")
                s.root_used = sem(name + "_root_used")
                s.var_ready, s.std_ready = sem(name + "_var_ready"), sem(name + "_std_ready")
                s.turned = sem(name + "_turned")
                s.copied = sem(name + "_copied")
                s.product = sem(name + "_product")
                s.msg_made, s.root_made = sem(name + "_msg_made"), sem(name + "_root_made")
                s.stored = sems(name + "_stored", 2)
                s.own = sem(name + "_own")

        class EdgePhase:
            def __init__(s, name):
                s.name = name
                s.attr_loaded, s.ids_loaded = sems(name + "_attr_loaded", RING), sems(name + "_ids_loaded", RING)
                s.gathered, s.stored = sems(name + "_gathered", RING), sems(name + "_stored", RING)
                s.turned = sem(name + "_turned")
                s.copied = sem(name + "_copied")
                s.msg_ready = sem(name + "_msg_ready")
                s.columns = sem(name + "_columns")
                s.own = sem(name + "_own")
                s.pen_ready = sem(name + "_pen_ready")
                s.seam_gathered, s.seam_maxed = sem(name + "_seam_gathered"), sem(name + "_seam_maxed")
                s.seam_stored = sem(name + "_seam_stored")
                s.last_turned, s.carried, s.carry_turned = (
                    sem(name + "_last_turned"), sem(name + "_carried"), sem(name + "_carry_turned"))

        def apart(engine):
            engine.sem_inc(waits_met, 1)

        norm, mid, fin = NodePhase("norm"), NodePhase("mid"), NodePhase("fin")
        edges = [EdgePhase("edge0"), EdgePhase("edge1")]

        block = ctx.enter_context(nc.Block())

        @block.sync
        def _(sp):
            x_groups = by_group(x)

            def norm_loads(it):
                for b in range(2):
                    wait_slot(sp, norm.turned, NT * (2 * it + b - 1))
                    sp.dma_start(node_in[:, b, :], x_groups[:, 2 * it + b, :]).then_inc(norm.loaded[b], 16)

            norm_loads(0)
            with sp.Fori(1, NG // 2) as it:
                norm_loads(it)

            def edge_loads(ph, i, c):
                wait_slot(sp, ph.gathered[c], 16 * T * i)
                sp.dma_start(ids[:, c, :], src_chunks[:, RING * i + c, :]).then_inc(ph.ids_loaded[c], 16)
                wait_slot(sp, ph.turned, 2 * (RING * (i - 1) + c + 1))
                sp.dma_start(attr[:, c, :], attr_chunks[:, RING * i + c, :]).then_inc(ph.attr_loaded[c], 16)

            def edge_store(ph, i, c):
                sp.wait_ge(ph.columns, T * (RING * i + c + 1))
                sp.dma_start(run_chunks[:, RING * i + c, :], run[:, c, :]).then_inc(ph.stored[c], 16)

            def edge_pass(ph):
                for c in range(RING):
                    edge_loads(ph, 0, c)
                with sp.Fori(1, STEPS) as i:
                    for c in range(RING):
                        edge_loads(ph, i, c)
                        edge_store(ph, i - 1, c)
                for c in range(RING):
                    edge_store(ph, STEPS - 1, c)

            def node_loads(ph, layer, with_x):
                groups = by_group(root_table[layer])

                def loads(it):
                    for b in range(2):
                        wait_slot(sp, ph.gathered[b], 16 * GT * it)
                        sp.dma_start(end_ids[:, b, :], end_groups[:, 2 * it + b, :]).then_inc(ph.ids_loaded[b], 16)
                        wait_slot(sp, ph.root_used, 2 * it + b - 1)
                        sp.dma_start(root_in[:, b, :], groups[:, 2 * it + b, :]).then_inc(ph.loaded[b], 16)
                        if with_x:
                            sp.dma_start(msg_out[:, b, :], x_groups[:, 2 * it + b, :]).then_inc(ph.loaded[b], 16)

                loads(0)
                with sp.Fori(1, NG // 2) as it:
                    loads(it)

            edge_pass(edges[0])
            sp.wait_ge(ends_ready, 1)
            sp.dma_start(end_rows, ends_i[:, :]).then_inc(ends_stored, 16)
            sp.wait_ge(ends_stored, 16)
            for b in range(2):
                sp.wait_ge(norm.stored[b], 16 * NG)
            node_loads(mid, 0, False)
            edge_pass(edges[1])
            for b in range(2):
                sp.wait_ge(mid.stored[b], 16 * NG)
            node_loads(fin, 1, True)
            for b in range(2):
                sp.wait_ge(fin.stored[b], 8 * NG)

        @block.gpsimd
        def _(pool):
            pool.memset(ident[:, :], 0.0).then_inc(iotas, 1)
            pool.memset(before[:, :], 1.0).then_inc(iotas, 1)
            pool.iota(iota_i[:, :], [[1, P]], base=0, channel_multiplier=0).then_inc(iotas, 1)
            pool.iota(part_i[:, :], [[1, 1]], base=0, channel_multiplier=1).then_inc(iotas, 1)
            pool.wait_ge(iotas, 4)
            pool.affine_select(out=ident[:, :], in_=ident[:, :], compare_op=ALU.not_equal, fill=1.0, base=0,
                               pattern=[[-1, P]], channel_multiplier=1).then_inc(iotas, 1)
            pool.affine_select(out=before[:, :], in_=before[:, :], compare_op=ALU.is_gt, fill=0.0, base=0,
                               pattern=[[1, P]], channel_multiplier=-1).then_inc(iotas, 1)

            def gather_edges(ph, table, tables_stored):
                for b in range(2):
                    pool.wait_ge(tables_stored[b], 16 * NG)

                def step(i):
                    for c in range(RING):
                        pool.wait_ge(ph.ids_loaded[c], 16 * (i + 1))
                        wait_slot(pool, ph.msg_ready, NQ * (RING * (i - 1) + c + 1))
                        apart(pool)
                        for t in range(T):
                            pool.indirect_dma_start(
                                out=rows[:, c, t * D:(t + 1) * D], out_offset=None, in_=table,
                                in_offset=bass.IndirectOffsetOnAxis(ap=ids[:, c, t:t + 1], axis=0),
                            ).then_inc(ph.gathered[c], 16)

                step(0)
                with pool.Fori(1, STEPS) as i:
                    step(i)

            def mend_seams(ph):
                for c in range(RING):
                    pool.wait_ge(ph.stored[c], 16 * STEPS)
                pool.wait_ge(zero_stored, 32)
                pool.indirect_dma_start(out=seam_rows[:, :], out_offset=None, in_=run_rows,
                                        in_offset=bass.IndirectOffsetOnAxis(ap=seam_ids[:, 0:1], axis=0),
                                        ).then_inc(ph.seam_gathered, 16)
                pool.wait_ge(ph.seam_maxed, 1)
                pool.indirect_dma_start(out=run_rows,
                                        out_offset=bass.IndirectOffsetOnAxis(ap=seam_ids[:, 0:1], axis=0),
                                        in_=seam_max[:, :], in_offset=None).then_inc(ph.seam_stored, 16)
                pool.wait_ge(ph.seam_stored, 16)

            def gather_nodes(ph, freed, per_group):
                def step(it):
                    for b in range(2):
                        pool.wait_ge(ph.ids_loaded[b], 16 * (it + 1))
                        wait_slot(pool, freed, per_group * (2 * it + b - 1))
                        apart(pool)
                        for j in range(GT):
                            pool.indirect_dma_start(
                                out=node_in[:, b, j * D:(j + 1) * D], out_offset=None, in_=run_rows,
                                in_offset=bass.IndirectOffsetOnAxis(ap=end_ids[:, b, j:j + 1], axis=0),
                            ).then_inc(ph.gathered[b], 16)

                step(0)
                with pool.Fori(1, NG // 2) as it:
                    step(it)

            gather_edges(edges[0], msg_table[0], norm.stored)
            mend_seams(edges[0])
            gather_nodes(mid, mid.turned, NT)
            gather_edges(edges[1], msg_table[1], mid.stored)
            mend_seams(edges[1])
            gather_nodes(fin, fin.ready, 1)

        @block.tensor
        def _(pe):
            def transform(ph, layer):
                def step(it):
                    for b in range(2):
                        q = 2 * it + b
                        pe.wait_ge(ph.ready, q + 1)
                        wait_slot(pe, ph.copied, NT * q)
                        j = 0
                        for n, tiles in enumerate(TP_BANKS):
                            for s in range(tiles):
                                tr = pe.transpose(turn[n][0:D, s * NP:(s + 1) * NP],
                                                  node_in[:, b, j * D:(j + 1) * D], ident[0:NP, 0:NP])
                                j += 1
                            tr.then_inc(ph.turned, 1)
                        pe.wait_ge(ph.copied, NT * (q + 1))
                        wait_slot(pe, ph.msg_made, HALVES * q)
                        wait_slot(pe, ph.root_made, HALVES * q)
                        for n in range(2 * HALVES):
                            for s in range(HT):
                                j = n // 2 * HT + s
                                mm = pe.matmul(bank[n][0:NP, s * D:(s + 1) * D], node_t[:, j * NP:(j + 1) * NP],
                                               w_node[layer][:, (n % 2) * D:(n % 2 + 1) * D], start=True, stop=True)
                            mm.then_inc(ph.product, 1)

                step(0)
                with pe.Fori(1, NG // 2) as it:
                    step(it)

            def edge_pass(ph, layer):
                def step(i):
                    for c in range(RING):
                        k = RING * i + c
                        pe.wait_ge(ph.attr_loaded[c], 16 * (i + 1))
                        wait_slot(pe, ph.copied, 3 * k)
                        for g, (t, n) in enumerate(QUADS):
                            into = turn_a if g < 4 else turn_b
                            tr = pe.transpose(into[0:n * DE, (g % 4) * P:(g % 4 + 1) * P],
                                              attr[:, c, t * DE:(t + n) * DE], ident[:, :])
                            if g in (3, NQ - 1):
                                tr.then_inc(ph.turned, 1)
                        if layer == 0:
                            pe.wait_ge(hot_made, k + 1)
                            wait_slot(pe, hist_added, k)
                            for t in range(T):
                                mm = pe.matmul(spare_bank[0:NP, 0:NODES], hot_p[:, t, :], hot_j[:, t, :],
                                               start=(t == 0), stop=(t == T - 1))
                            mm.then_inc(hist_done, 1)
                        pe.wait_ge(ph.copied, 3 * (k + 1))
                        pe.wait_ge(ph.gathered[c], 16 * T * (i + 1))
                        for g, (t, n) in enumerate(QUADS):
                            to = bank[(NQ * c + g) % BANKS][:, 0:n * D]
                            wait_slot(pe, ph.columns, T * k + freed_columns(g))
                            pe.matmul(to, attr_t[0:n * DE, c, g * P:(g + 1) * P], w_blocks[layer][0:n * DE, 0:n * D],
                                      start=True, stop=False)
                            mm = pe.matmul(to, ident[:, :], rows[:, c, t * D:(t + n) * D], start=False, stop=True)
                            mm.then_inc(ph.msg_ready, 1)

                step(0)
                with pe.Fori(1, STEPS) as i:
                    step(i)

            def turn_seams(ph):
                pe.wait_ge(ph.columns, EPP)
                pe.transpose(turn_a[0:D, 0:P], run[:, RING - 1, (T - 1) * D:T * D], ident[:, :]).then_inc(ph.last_turned, 1)
                pe.wait_ge(ph.carried, 1)
                pe.transpose(turn_b[:, 0:D], carry[:, 0:P], ident[0:D, 0:D]).then_inc(ph.carry_turned, 1)

            pe.wait_ge(iotas, 6)
            pe.wait_ge(w_loaded, 16 * 6)
            transform(norm, 0)
            pe.wait_ge(blocks_loaded, 16 * 8)
            pe.wait_ge(norm.msg_made, HALVES * NG)
            pe.wait_ge(norm.root_made, HALVES * NG)
            pe.wait_ge(consts_made, 1)
            pe.transpose(turn_a[0:D, 0:P], seam_pen[:, :], ident[:, :]).then_inc(seam_turned, 1)
            pe.wait_ge(seam_turned, 1)
            pe.wait_ge(consts_made, 2)
            edge_pass(edges[0], 0)
            pe.wait_ge(ends_counted, 1)
            pe.matmul(spare_bank[0:NP, 0:1], before[0:NP, 0:NP], hist_sum[:, :], start=True, stop=True
                      ).then_inc(ends_counted, 1)
            turn_seams(edges[0])
            transform(mid, 1)
            pe.wait_ge(mid.msg_made, HALVES * NG)
            pe.wait_ge(mid.root_made, HALVES * NG)
            edge_pass(edges[1], 1)
            turn_seams(edges[1])

        @block.scalar
        def _(act):
            for l in range(2):
                act.dma_start(w_node[l][:, 0:D], w_msg[l]).then_inc(w_loaded, 16)
                act.dma_start(w_node[l][:, D:2 * D], w_root[l]).then_inc(w_loaded, 16)
                act.dma_start(bias_rep[l][:, :], bias[l].partition_broadcast(NP)).then_inc(w_loaded, 16)
            act.dma_start(dst_i, dst_rows).then_inc(dst_loaded, 16)
            act.wait_ge(zeros_made, 2)
            with nc.allow_non_contiguous_dma(reason="one column, once"):
                act.dma_start(edge_ids[:, 0:1], dst_rows[:, 0:1]).then_inc(dst_loaded, 16)
                act.dma_start(edge_ids[:, 1:2], dst_rows[:, EPP - 1:EPP]).then_inc(dst_loaded, 16)
                act.dma_start(edge_ids[1:P, 2:3], dst_rows[0:P - 1, EPP - 1:EPP]).then_inc(dst_loaded, 16)
                act.dma_start(edge_ids[0:P - 1, 3:4], dst_rows[1:P, 0:1]).then_inc(dst_loaded, 16)
            for z in range(2):
                act.dma_start(run_rows[E + z * P:E + (z + 1) * P, :], seam_max[:, :]).then_inc(zero_stored, 16)
            act.wait_ge(blocks_zero, 2)
            for l in range(2):
                for g in range(4):
                    act.dma_start(w_blocks[l][g * DE:(g + 1) * DE, g * D:(g + 1) * D], w_edge[l]
                                  ).then_inc(blocks_loaded, 16)

            def deviation(q):
                act.wait_ge(norm.var_ready, q + 1)
                act.activation(std[:, :], moments[:, :, 1], ACT.Sqrt, bias=eps[0:NP, :]).then_inc(norm.std_ready, 1)

            def tables(ph, msgs, roots, it, b):
                q = 2 * it + b
                wait_slot(act, ph.product, 2 * HALVES * q)
                at = 0
                for n, tiles in enumerate(TP_BANKS):
                    act.wait_ge(ph.turned, NT * q + n + 1)
                    act.copy(node_t[:, at * NP:(at + tiles) * NP], turn[n][0:D, 0:tiles * NP]
                             ).then_inc(ph.copied, 1)
                    at += tiles
                wait_slot(act, ph.stored[b], 32 * it)
                for h in range(HALVES):
                    act.wait_ge(ph.product, 2 * HALVES * q + 2 * h + 1)
                    act.copy(msg_out[:, b, h * HT * D:(h + 1) * HT * D], bank[2 * h][0:NP, 0:HT * D]
                             ).then_inc(ph.msg_made, 1)
                act.wait_ge(ph.msg_made, HALVES * (q + 1))
                act.dma_start(msgs[:, q, :], msg_out[:, b, :]).then_inc(ph.stored[b], 16)
                act.wait_ge(ph.root_made, HALVES * (q + 1))
                act.dma_start(roots[:, q, :], root_out[:, b, :]).then_inc(ph.stored[b], 16)

            def transform(ph, layer):
                groups = ph, by_group(msg_table[layer]), by_group(root_table[layer])
                if ph is norm:
                    def step(it):
                        for b in range(2):
                            deviation(2 * it + b + 1)
                            tables(*groups, it, b)

                    deviation(0)
                    step(0)
                    with act.Fori(1, NG // 2 - 1) as it:
                        step(it)
                    deviation(NG - 1)
                    tables(*groups, NG // 2 - 1, 0)
                    tables(*groups, NG // 2 - 1, 1)
                    return
                for b in range(2):
                    tables(*groups, 0, b)
                with act.Fori(1, NG // 2) as it:
                    for b in range(2):
                        tables(*groups, it, b)

            def edge_pass(ph):
                def step(i):
                    for c in range(RING):
                        k = RING * i + c
                        wait_slot(act, ph.msg_ready, NQ * (k - RING + 1))
                        act.wait_ge(ph.turned, 2 * k + 1)
                        act.copy(attr_t[:, c, 0:4 * P], turn_a[:, 0:4 * P]).then_inc(ph.copied, 1)
                        act.wait_ge(ph.turned, 2 * k + 2)
                        act.copy(attr_t[:, c, 4 * P:(NQ - 1) * P], turn_b[:, 0:(NQ - 5) * P]).then_inc(ph.copied, 1)
                        act.copy(attr_t[0:DE, c, (NQ - 1) * P:NQ * P], turn_b[0:DE, (NQ - 5) * P:(NQ - 4) * P]
                                 ).then_inc(ph.copied, 1)

                step(0)
                with act.Fori(1, STEPS) as i:
                    step(i)

            transform(norm, 0)
            edge_pass(edges[0])
            transform(mid, 1)
            edge_pass(edges[1])
            outs = by_group(out)
            with act.Fori(0, NG // 2) as it:
                for b in range(2):
                    act.wait_ge(fin.ready, 2 * it + b + 1)
                    act.dma_start(outs[:, 2 * it + b, :], root_out[:, b, :]).then_inc(fin.stored[b], 16)

        @block.vector
        def _(dve):
            done = [0]

            def own(ins):
                ins.then_inc(vec, 1)
                done[0] += 1
                dve.wait_ge(vec, done[0])

            dve.memset(seam_max[:, :], 0.0).then_inc(zeros_made, 1)
            dve.memset(edge_ids[:, :], -1).then_inc(zeros_made, 1)
            for l in range(2):
                dve.memset(w_blocks[l][:, :], 0.0).then_inc(blocks_zero, 1)
            own(dve.memset(eps[:, :], EPS))

            def normed(it, b):
                q = 2 * it + b
                o = 3 * q
                dve.wait_ge(norm.loaded[b], 16 * (it + 1))
                for j in range(GT):
                    ins = dve.bn_stats(stats[:, j, :], node_in[:, b, j * D:(j + 1) * D])
                ins.then_inc(norm.own, 1)
                dve.wait_ge(norm.own, o + 1)
                apart(dve)
                for j in range(GT):
                    ins = dve.bn_aggr(moments[:, j, :], stats[:, j, :])
                ins.then_inc(norm.var_ready, 1)
                dve.wait_ge(norm.std_ready, q + 1)
                dve.reciprocal(rstd[:, :], std[:, :]).then_inc(norm.own, 1)
                dve.wait_ge(norm.own, o + 2)
                for j in range(GT):
                    one = node_in[:, b, j * D:(j + 1) * D]
                    ins = dve.tensor_scalar(one, one, moments[:, j, 0:1], rstd[:, j:j + 1], ALU.subtract, ALU.mult)
                ins.then_inc(norm.own, 1)
                dve.wait_ge(norm.own, o + 3)
                dve.tensor_scalar(node_in[:, b, :], node_in[:, b, :], 0.0, None, ALU.max).then_inc(norm.ready, 1)

            def combined(ph, it, b):
                q = 2 * it + b
                dve.wait_ge(ph.loaded[b], (32 if ph is fin else 16) * (it + 1))
                dve.wait_ge(ph.gathered[b], 16 * GT * (it + 1))
                dve.tensor_tensor(root_in[:, b, :], node_in[:, b, :], root_in[:, b, :], ALU.add).then_inc(ph.own, 1)
                dve.wait_ge(ph.own, (2 if ph is fin else 1) * q + 1)
                if ph is mid:
                    dve.scalar_tensor_tensor(out=node_in[:, b, :], in0=root_in[:, b, :], scalar=SLOPE,
                                             in1=root_in[:, b, :], op0=ALU.mult, op1=ALU.max
                                             ).then_inc(ph.ready, 1)
                    dve.wait_ge(ph.ready, q + 1)
                    dve.sem_inc(ph.root_used, 1)
                    return
                dve.scalar_tensor_tensor(out=root_in[:, b, :], in0=root_in[:, b, :], scalar=SLOPE,
                                         in1=root_in[:, b, :], op0=ALU.mult, op1=ALU.max).then_inc(ph.own, 1)
                dve.wait_ge(ph.own, 2 * q + 2)
                wait_slot(dve, ph.stored[b], 16 * it)
                dve.tensor_tensor(root_out[:, b, :], root_in[:, b, :], msg_out[:, b, :], ALU.add
                                  ).then_inc(ph.ready, 1)
                dve.wait_ge(ph.ready, q + 1)
                dve.sem_inc(ph.root_used, 1)

            def rooted(ph, layer, it, b):
                q = 2 * it + b
                wait_slot(dve, ph.stored[b], 32 * it)
                for h in range(HALVES):
                    dve.wait_ge(ph.product, 2 * HALVES * q + 2 * h + 2)
                    dve.tensor_tensor(root_out[:, b, h * HT * D:(h + 1) * HT * D].rearrange("p (s f) -> p s f", s=HT),
                                      bank[2 * h + 1][0:NP, 0:HT * D].rearrange("p (s f) -> p s f", s=HT),
                                      bias_rep[layer][:, :].unsqueeze(1).to_broadcast([NP, HT, D]), ALU.add
                                      ).then_inc(ph.root_made, 1)

            def transform(ph, layer, make):
                def step(it):
                    make(it, 1)
                    rooted(ph, layer, it, 0)
                    make(it + 1, 0)
                    rooted(ph, layer, it, 1)

                make(0, 0)
                step(0)
                with dve.Fori(1, NG // 2 - 1) as it:
                    step(it)
                make(NG // 2 - 1, 1)
                rooted(ph, layer, NG // 2 - 1, 0)
                rooted(ph, layer, NG // 2 - 1, 1)

            def prepare_edges():
                dve.wait_ge(iotas, 6)
                dve.tensor_copy(iota_b[:, :], iota_i[:, :])
                dve.wait_ge(dst_loaded, 16 * 5)
                dve.memset(penalty[:, 0:1], 0.0)
                dve.tensor_copy(edge_f[:, :], edge_ids[:, :])
                own(dve.tensor_copy(dst_f, dst_i))
                dve.tensor_tensor(penalty[:, 1:EPP], dst_f[:, 1:EPP], dst_f[:, 0:EPP - 1], ALU.not_equal)
                own(dve.tensor_scalar(tmp_f, dst_f, edge_f[:, 0:1], None, ALU.is_equal))
                dve.tensor_scalar(penalty[:, 1:EPP], penalty[:, 1:EPP], LOW, None, ALU.mult)
                own(dve.tensor_reduce(seam[:, 0:1], tmp_f, AX.X, ALU.add))
                own(dve.tensor_scalar(tmp_f, dst_f, -(NODES - 1) / 2, 1.0 / NODES, ALU.add, ALU.mult))
                own(dve.tensor_scalar(tmp_f, tmp_f, 1.5 * 2 ** 23, -1.5 * 2 ** 23, ALU.add, ALU.add))
                dve.tensor_copy(node_p[:, :], tmp_f)
                own(dve.scalar_tensor_tensor(out=node_j[:, :], in0=tmp_f, scalar=-float(NODES), in1=dst_f,
                                             op0=ALU.mult, op1=ALU.add))
                first, last, prev, nxt = (edge_f[:, n:n + 1] for n in range(4))
                length, open_, ends_here, at = (seam[:, n:n + 1] for n in range(4))
                differs, spare, shift, part = (seam[:, n:n + 1] for n in range(4, 8))
                dve.tensor_copy(part, part_i[:, :])
                dve.tensor_tensor(open_, prev, first, ALU.is_equal)
                dve.tensor_tensor(ends_here, last, first, ALU.not_equal)
                own(dve.tensor_tensor(differs, nxt, first, ALU.not_equal))
                dve.tensor_scalar(spare, part, float(SPARE), None, ALU.add)
                own(dve.tensor_tensor(ends_here, ends_here, differs, ALU.max))
                own(dve.tensor_tensor(open_, open_, ends_here, ALU.mult))
                own(dve.scalar_tensor_tensor(out=shift, in0=part, scalar=float(EPP - 1), in1=length,
                                             op0=ALU.mult, op1=ALU.add))
                own(dve.tensor_scalar(shift, shift, -1.0 - SPARE, None, ALU.add))
                own(dve.tensor_tensor(at, shift, open_, ALU.mult))
                own(dve.tensor_tensor(at, at, spare, ALU.add))
                dve.tensor_copy(seam_ids[:, :], at)
                own(dve.tensor_tensor(differs, last, prev, ALU.not_equal))
                own(dve.tensor_scalar(differs, differs, LOW, None, ALU.mult))
                dve.tensor_copy(seam_pen[:, :], differs.to_broadcast([P, D])).then_inc(consts_made, 1)
                dve.memset(hist[:, :], 0.0)
                dve.memset(carry[:, 0:1], LOW)
                dve.wait_ge(seam_turned, 1)
                dve.tensor_copy(seam_pen_t[:, :], turn_a[0:D, 0:P]).then_inc(consts_made, 1)

            def edge_pass(ph, layer):
                own(dve.memset(run[:, RING - 1, (T - 1) * D:T * D], LOW))

                def step(i):
                    for c in range(RING):
                        k = RING * i + c
                        wait_slot(dve, ph.columns, T * k)
                        dve.tensor_copy(pen[:, :], penalty[:, bass.ds(T * k, T)]).then_inc(ph.pen_ready, 1)
                        if layer == 0:
                            wait_slot(dve, hist_done, k)
                            dve.tensor_tensor(
                                hot_p, iota_b[:, 0:NP].unsqueeze(1).to_broadcast([P, T, NP]),
                                node_p[:, bass.ds(T * k, T)].unsqueeze(2).to_broadcast([P, T, NP]), ALU.is_equal)
                            dve.tensor_tensor(
                                hot_j, iota_b[:, 0:NODES].unsqueeze(1).to_broadcast([P, T, NODES]),
                                node_j[:, bass.ds(T * k, T)].unsqueeze(2).to_broadcast([P, T, NODES]), ALU.is_equal
                            ).then_inc(hot_made, 1)
                        dve.wait_ge(ph.pen_ready, k + 1)
                        wait_slot(dve, ph.stored[c], 16 * i)
                        for t in range(T):
                            g, s = t // 4, t % 4
                            if s == 0:
                                dve.wait_ge(ph.msg_ready, NQ * k + g + 1)
                            if t:
                                dve.wait_ge(ph.columns, T * k + t)
                            was = run[:, c, (t - 1) * D:t * D] if t else run[:, (c - 1) % RING, (T - 1) * D:T * D]
                            dve.scalar_tensor_tensor(
                                out=run[:, c, t * D:(t + 1) * D], in0=was, scalar=pen[:, t:t + 1],
                                in1=bank[(NQ * c + g) % BANKS][:, s * D:(s + 1) * D], op0=ALU.add, op1=ALU.max
                            ).then_inc(ph.columns, 1)
                        if layer == 0:
                            dve.wait_ge(hist_done, k + 1)
                            dve.tensor_tensor(hist[:, :], hist[:, :], spare_bank[0:NP, 0:NODES], ALU.add
                                              ).then_inc(hist_added, 1)

                step(0)
                with dve.Fori(1, STEPS) as i:
                    step(i)

            def mend_seams(ph):
                dve.wait_ge(ph.last_turned, 1)
                dve.tensor_tensor_scan(carry[:, 1:1 + P], seam_pen_t[:, :], turn_a[0:D, 0:P], LOW,
                                       ALU.add, ALU.max).then_inc(ph.carried, 1)
                dve.wait_ge(ph.carry_turned, 1)
                dve.wait_ge(ph.seam_gathered, 16)
                dve.tensor_tensor(seam_max[:, :], seam_rows[:, :], turn_b[:, 0:D], ALU.max).then_inc(ph.seam_maxed, 1)

            def count_ends():
                dve.wait_ge(hist_added, STEPS * RING)
                dve.tensor_reduce(hist_sum[:, :], hist[:, :], AX.X, ALU.add).then_inc(ends_counted, 1)
                dve.memset(some[:, :], 1.0)
                dve.wait_ge(ends_counted, 2)
                own(dve.tensor_copy(hist_before[:, :], spare_bank[0:NP, 0:1]))
                own(dve.tensor_tensor_scan(ends[:, :], some[:, :], hist[:, :], hist_before[:, 0:1],
                                           ALU.mult, ALU.add))
                dve.tensor_scalar(ends[:, :], ends[:, :], -1.0 - ZERO, None, ALU.add)
                own(dve.tensor_scalar(some[:, :], hist[:, :], 1.0, None, ALU.min))
                own(dve.tensor_tensor(ends[:, :], ends[:, :], some[:, :], ALU.mult))
                dve.tensor_scalar(ends_i[:, :], ends[:, :], float(ZERO), None, ALU.add).then_inc(ends_ready, 1)

            transform(norm, 0, normed)
            prepare_edges()
            edge_pass(edges[0], 0)
            count_ends()
            mend_seams(edges[0])
            transform(mid, 1, lambda it, b: combined(mid, it, b))
            edge_pass(edges[1], 1)
            mend_seams(edges[1])
            for b in range(2):
                combined(fin, 0, b)
            with dve.Fori(1, NG // 2) as it:
                for b in range(2):
                    combined(fin, it, b)


INPUTS = ["x", "src", "dst", "edge_attr_32", "L0_gnn_W1_msg", "L0_gnn_W1_edge", "L0_gnn_W1_root", "L0_gnn_b1",
          "L0_gnn_W2_msg", "L0_gnn_W2_edge", "L0_gnn_W2_root", "L0_gnn_b2"]


def kernel(**inputs):
    import concourse.bacc as bacc
    from concourse.bass_utils import run_bass_kernel_spmd

    nc = bacc.Bacc("TRN2", target_bir_lowering=False, num_devices=1)
    arrays, aps = {}, {}
    for name in INPUTS:
        a = np.ascontiguousarray(inputs[name])
        arrays[f"in_{name}"] = a
        aps[name] = nc.dram_tensor(f"in_{name}", a.shape, mybir.dt.from_np(a.dtype), kind="ExternalInput").ap()
    out = nc.dram_tensor("out", (N, D), F32, kind="ExternalOutput").ap()
    layer = lambda what: [aps[f"L0_gnn_{what.format(n)}"] for n in (1, 2)]
    build(nc, aps["x"], aps["src"], aps["dst"], aps["edge_attr_32"],
          layer("W{}_msg"), layer("W{}_edge"), layer("W{}_root"), layer("b{}"), out)
    r = run_bass_kernel_spmd(nc, [arrays], core_ids=[0])
    return r.results[0]["out"]
```

```python
from contextlib import ExitStack

import numpy as np

import concourse.bass as bass
from concourse import mybir
from concourse.alu_op_type import AluOpType as ALU

F32 = mybir.dt.float32
BF16 = mybir.dt.bfloat16
I32 = mybir.dt.int32
ACT = mybir.ActivationFunctionType
AX = mybir.AxisListType

P = 128
N, D = 12500, 96
E, DE = 400000, 32
EPS = 1e-5
SLOPE = 0.01
LOW = -3.0e38

NP = 125
NODES = N // NP
WIDE = NP // 16 * 16
GT = 5
NG = NODES // GT
NR = 4
NSTEPS = NG // NR
TP_BANKS = [3, 2]
NT = len(TP_BANKS)
COPIES_AT = [sum(TP_BANKS[:n]) for n in range(NT)]
AHEAD = 3
POOL_TILES = 2

EPP = E // P
T = 25
RING = 5
STEPS = EPP // (T * RING)
QUADS = [(4 * g, min(4, T - 4 * g)) for g in range((T + 3) // 4)]
NQ = len(QUADS)
TAIL = T - 5
HOTS_LAST, HISTOGRAM_LAST = 3, 5
BANK_OF = [0, 1, 2, 3, 0, 1, 2]

SPARE = E
ZERO = E + P
ROWS = E + 2 * P


def wait_slot(engine, semaphore, count):
    if not isinstance(count, int) or count > 0:
        engine.wait_ge(semaphore, count)


def freed_columns(g):
    last = max(h for h in range(g - NQ, g) if BANK_OF[h % NQ] == BANK_OF[g])
    return min(4 * (last + 1), T) if last >= 0 else min(4 * (last + NQ + 1), T) - T


assert NP * NODES == N and NG * GT == NODES and sum(TP_BANKS) == GT and NR % 2 == 0 and NSTEPS * NR == NG
assert P * EPP == E and STEPS * RING * T == EPP and len(BANK_OF) == NQ and T % 4 == 1


def build(nc, x, src, dst, edge_attr, w_msg, w_edge, w_root, bias, out):
    with ExitStack() as ctx:
        def sb(name, shape, dt=F32):
            return ctx.enter_context(nc.sbuf_tensor(name, shape, dt))

        def ps(name):
            return ctx.enter_context(nc.psum_tensor(name, [P, 512], F32))

        def sem(name):
            return ctx.enter_context(nc.semaphore(name))

        def sems(name, n):
            return [sem(f"{name}{i}") for i in range(n)]

        msg_table = [nc.dram_tensor(f"msg_table{l}", (N, D), F32).ap() for l in range(2)]
        turned_rows = [nc.dram_tensor(f"turned_rows{l}", (NG, D, GT * NP), F32).ap() for l in range(2)]
        run_rows = nc.dram_tensor("run_rows", (ROWS, D), F32).ap()

        def by_group(a):
            return a.rearrange("(p q j) f -> p q (j f)", p=NP, q=NG)

        def by_chunk(a):
            return a.rearrange("(p k t) f -> p k (t f)", p=P, t=T)

        src_chunks = src.rearrange("(p k t) -> p k t", p=P, t=T)
        dst_rows = dst.rearrange("(p e) -> p e", p=P)
        attr_chunks = by_chunk(edge_attr)
        run_chunks = by_chunk(run_rows[0:E, :])

        ident = sb("ident", [P, P])
        before = sb("before", [P, P])
        iota_i = sb("iota_i", [P, P], I32)
        part_i = sb("part_i", [P, 1], I32)
        w_msgs = [sb(f"w_msg{l}", [D, D]) for l in range(2)]
        w_roots = [sb(f"w_root{l}", [D + 1, D]) for l in range(2)]
        w_blocks = [sb(f"w_blocks{l}", [P, 4 * D]) for l in range(2)]
        eps, root_of_eps = sb("eps", [P, 1]), sb("root_of_eps", [P, 1])
        penalty = sb("penalty", [P, EPP])
        node_p = sb("node_p", [P, EPP], BF16)
        node_j = sb("node_j", [P, EPP], BF16)
        hot = sb("hot", [P, T * (NP + NODES) + 1], BF16)
        hot_p = hot[:, 0:T * NP].rearrange("p (t n) -> p t n", n=NP)
        hot_j = hot[:, T * NP + 1:T * (NP + NODES) + 1].rearrange("p (t n) -> p t n", n=NODES)
        rows = sb("rows", [P, RING, T * D])
        run = sb("run", [P, RING, T * D])
        attr = sb("attr", [P, RING, T * DE])
        attr_t = sb("attr_t", [P, RING, NQ * P])
        ids = sb("ids", [P, RING, T], I32)
        pen = sb("pen", [P, RING, T])
        x_in = rows[0:NP, 0:NR, 0:GT * D]
        node_in = sb("node_in", [P, NR, GT * D])
        msg_out = sb("msg_out", [NP, NR, GT * D])
        root_t = sb("root_t", [D + 1, NR, GT * NP])
        node_t = hot[0:D, 0:2 * NR * GT * NP].bitcast(F32).rearrange("p (b n) -> p b n", b=NR)
        end_ids = sb("end_ids", [P, NR, GT], I32)
        stats = sb("stats", [NP, 2, GT, 6])
        moments = sb("moments", [NP, 2, GT, 2])
        std = sb("std", [NP, 2, GT])
        rstd = sb("rstd", [NP, 2, GT])
        hist = sb("hist", [NP, NODES])
        hist_sum = sb("hist_sum", [NP, 1])
        hist_before = sb("hist_before", [NP, 1])
        ends = sb("ends", [NP, NODES])
        some = sb("some", [NP, NODES])
        edge_ids = sb("edge_ids", [P, 4], I32)
        edge_f = sb("edge_f", [P, 4])
        seam = sb("seam", [P, 8])
        seam_ids = sb("seam_ids", [P, 1], I32)
        seam_pen = sb("seam_pen", [P, D])
        seam_pen_t = sb("seam_pen_t", [D, P])
        carry = sb("carry", [D, 1 + P])
        seam_rows = sb("seam_rows", [P, D])
        seam_max = sb("seam_max", [P, D])
        dst_i = run[:, 0:2, :].rearrange("p c n -> p (c n)")[:, 0:EPP].bitcast(I32)
        dst_f = run[:, 2:4, :].rearrange("p c n -> p (c n)")[:, 0:EPP]
        tmp_f = run[:, 2:5, :].rearrange("p c n -> p (c n)")[:, EPP:2 * EPP]

        bank = [ps(f"bank{i}") for i in range(max(BANK_OF) + 1)]
        iota_bank = ps("iota_bank")
        turn_a, turn_b, spare_bank = ps("turn_a"), ps("turn_b"), ps("spare_bank")
        turn = [[turn_a, turn_b], [spare_bank, iota_bank]]

        iotas, w_loaded, blocks_zero = sem("iotas"), sem("w_loaded"), sem("blocks_zero")
        others_loaded, eps_made = sem("others_loaded"), sem("eps_made")
        consts_made, dst_loaded = sem("consts_made"), sem("dst_loaded")
        zero_stored, zeros_made = sem("zero_stored"), sem("zeros_made")
        waits_met = sem("waits_met")
        vec = sem("vec")
        rstd_made, pool_normed = sem("rstd_made"), sem("pool_normed")
        bn_made, var_ready, std_ready = sem("bn_made"), sem("var_ready"), sem("std_ready")
        x_loaded, activated_made = sems("x_loaded", NR), sem("activated_made")
        seam_turned, ends_counted = sem("seam_turned"), sem("ends_counted")
        ones_made = sem("ones_made")
        hot_made, hist_done, hist_added = sem("hot_made"), sem("hist_done"), sem("hist_added")

        class NodePhase:
            def __init__(s, name, gathers, tables):
                s.stored = sems(name + "_stored", NR)
                s.ready = sem(name + "_ready")
                if gathers:
                    s.loaded = sems(name + "_loaded", NR)
                    s.ids_made = sem(name + "_ids_made")
                    s.gathered = sems(name + "_gathered", NR)
                    s.root_ready = sem(name + "_root_ready")
                    s.summed = sem(name + "_summed")
                if tables:
                    s.turned = sem(name + "_turned")
                    s.copied = sem(name + "_copied")
                    s.product = sem(name + "_product")
                    s.msg_made = sem(name + "_msg_made")

        class EdgePhase:
            def __init__(s, name):
                s.attr_loaded, s.ids_loaded = sems(name + "_attr_loaded", RING), sems(name + "_ids_loaded", RING)
                s.gathered, s.stored = sems(name + "_gathered", RING), sems(name + "_stored", RING)
                s.last_gathered = sems(name + "_last_gathered", NQ)
                s.turned = sem(name + "_turned")
                s.copied = sem(name + "_copied")
                s.msg_ready = sem(name + "_msg_ready")
                s.columns = sem(name + "_columns")
                s.pen_ready = sem(name + "_pen_ready")
                s.seam_gathered, s.seam_maxed = sem(name + "_seam_gathered"), sem(name + "_seam_maxed")
                s.seam_stored = sem(name + "_seam_stored")
                s.last_turned, s.carried, s.carry_turned = (
                    sem(name + "_last_turned"), sem(name + "_carried"), sem(name + "_carry_turned"))

        def apart(engine):
            engine.sem_inc(waits_met, 1)

        def gathered_by(ph, last, c, t):
            return ph.last_gathered[t // 4] if last and c == RING - 1 else ph.gathered[c]

        def store_turned(engine, ph, layer, it, b):
            q = NR * it + b
            engine.wait_ge(ph.copied, NT * (q + 1))
            engine.dma_start(turned_rows[layer][q, :, :], node_t[:, b, :]).then_inc(ph.stored[b], 16)

        def store_msg_rows(engine, ph, layer, it, b):
            q = NR * it + b
            engine.wait_ge(ph.msg_made, q + 1)
            engine.dma_start(by_group(msg_table[layer])[:, q, :], msg_out[:, b, :]).then_inc(ph.stored[b], 16)

        norm = NodePhase("norm", gathers=False, tables=True)
        mid = NodePhase("mid", gathers=True, tables=True)
        fin = NodePhase("fin", gathers=True, tables=False)
        edges = [EdgePhase("edge0"), EdgePhase("edge1")]

        block = ctx.enter_context(nc.Block())

        @block.sync
        def _(sp):
            x_groups = by_group(x)

            def load_x(to, it, b):
                for part in (slice(0, WIDE), slice(WIDE, NP)):
                    sp.dma_start(to[part, :], x_groups[part, NR * it + b, :]).then_inc(x_loaded[b], 16)

            def norm_loads(it, stores):
                for b in range(NR):
                    wait_slot(sp, norm.ready, NR * (it - 1) + b + 1)
                    wait_slot(sp, pool_normed, NR * (it - 1) + b + 1)
                    load_x(x_in[:, b, :], it, b)
                    if stores:
                        store_turned(sp, norm, 0, it - 1, b)

            def ids_loads(ph, i, c):
                wait_slot(sp, ph.gathered[c], 16 * T * i)
                sp.dma_start(ids[:, c, :], src_chunks[:, RING * i + c, :]).then_inc(ph.ids_loaded[c], 16)

            def attr_loads(ph, i, c):
                wait_slot(sp, ph.turned, 2 * (RING * (i - 1) + c + 1))
                sp.dma_start(attr[:, c, :], attr_chunks[:, RING * i + c, :]).then_inc(ph.attr_loaded[c], 16)

            def edge_store(ph, i, c, first=0, last=T):
                sp.wait_ge(ph.columns, T * (RING * i + c) + last)
                sp.dma_start(run_chunks[:, RING * i + c, first * D:last * D], run[:, c, first * D:last * D]
                             ).then_inc(ph.stored[c], 16)

            def edge_pass(ph):
                for c in range(RING):
                    attr_loads(ph, 0, c)
                with sp.Fori(1, STEPS) as i:
                    for c in range(RING):
                        ids_loads(ph, i, c)
                        attr_loads(ph, i, c)
                        edge_store(ph, i - 1, c)
                for c in range(RING - 1):
                    edge_store(ph, STEPS - 1, c)
                edge_store(ph, STEPS - 1, RING - 1, 0, TAIL)
                edge_store(ph, STEPS - 1, RING - 1, TAIL, T)

            def node_loads(ph, layer, with_x):
                def loads(it):
                    for b in range(NR):
                        q = NR * it + b
                        wait_slot(sp, ph.root_ready, q - NR + 1)
                        sp.dma_start(root_t[0:D, b, :], turned_rows[layer][q, :, :]).then_inc(ph.loaded[b], 16)
                        if with_x:
                            wait_slot(sp, ph.stored[b], 16 * it)
                            load_x(msg_out[:, b, :], it, b)

                loads(0)
                with sp.Fori(1, NSTEPS) as it:
                    loads(it)

            norm_loads(0, False)
            with sp.Fori(1, NSTEPS) as it:
                norm_loads(it, True)
            for c in range(RING):
                ids_loads(edges[0], 0, c)
            for b in range(NR):
                store_turned(sp, norm, 0, NSTEPS - 1, b)
            for b in range(NR):
                sp.wait_ge(norm.stored[b], 32 * NSTEPS)
            edge_pass(edges[0])
            node_loads(mid, 0, False)
            for c in range(RING):
                ids_loads(edges[1], 0, c)
            edge_pass(edges[1])
            for b in range(NR):
                sp.wait_ge(mid.stored[b], 32 * NSTEPS)
            node_loads(fin, 1, True)
            for b in range(NR):
                sp.wait_ge(fin.stored[b], 16 * NSTEPS)

        @block.gpsimd
        def _(pool):
            pool.memset(ident[:, :], 0.0).then_inc(iotas, 1)
            pool.memset(before[:, :], 1.0).then_inc(iotas, 1)
            pool.iota(iota_i[:, :], [[1, P]], base=0, channel_multiplier=0).then_inc(iotas, 1)
            pool.iota(part_i[:, :], [[1, 1]], base=0, channel_multiplier=1).then_inc(iotas, 1)
            pool.wait_ge(iotas, 4)
            pool.affine_select(out=ident[:, :], in_=ident[:, :], compare_op=ALU.not_equal, fill=1.0, base=0,
                               pattern=[[-1, P]], channel_multiplier=1).then_inc(iotas, 1)
            pool.affine_select(out=before[:, :], in_=before[:, :], compare_op=ALU.is_gt, fill=0.0, base=0,
                               pattern=[[1, P]], channel_multiplier=-1).then_inc(iotas, 1)

            def norm_tiles(it, b):
                pool.wait_ge(rstd_made, NR * it + b + 1)
                wait_slot(pool, norm.turned, NT * (NR * (it - 1) + b + 1))
                apart(pool)
                for j in range(GT - POOL_TILES, GT):
                    ins = pool.tensor_scalar(node_in[0:NP, b, j * D:(j + 1) * D], x_in[:, b, j * D:(j + 1) * D],
                                             moments[:, b % 2, j, 0:1], rstd[:, b % 2, j:j + 1],
                                             ALU.subtract, ALU.mult)
                ins.then_inc(pool_normed, 1)

            for b in range(NR):
                norm_tiles(0, b)
            with pool.Fori(1, NSTEPS) as it:
                for b in range(NR):
                    norm_tiles(it, b)

            def gather_edges(ph, table, tables_stored):
                for b in range(NR):
                    pool.wait_ge(tables_stored[b], 32 * NSTEPS)

                def step(i, last=False):
                    for c in range(RING):
                        pool.wait_ge(ph.ids_loaded[c], 16 * (i + 1))
                        wait_slot(pool, ph.msg_ready, NQ * (RING * (i - 1) + c + 1))
                        apart(pool)
                        for t in range(T):
                            pool.indirect_dma_start(
                                out=rows[:, c, t * D:(t + 1) * D], out_offset=None, in_=table,
                                in_offset=bass.IndirectOffsetOnAxis(ap=ids[:, c, t:t + 1], axis=0),
                            ).then_inc(gathered_by(ph, last, c, t), 16)

                step(0)
                with pool.Fori(1, STEPS - 1) as i:
                    step(i)
                step(STEPS - 1, last=True)

            def mend_seams(ph):
                for c in range(RING):
                    pool.wait_ge(ph.stored[c], 16 * (STEPS + (c == RING - 1)))
                pool.wait_ge(zero_stored, 32)
                pool.indirect_dma_start(out=seam_rows[:, :], out_offset=None, in_=run_rows,
                                        in_offset=bass.IndirectOffsetOnAxis(ap=seam_ids[:, 0:1], axis=0),
                                        ).then_inc(ph.seam_gathered, 16)
                pool.wait_ge(ph.seam_maxed, 1)
                pool.indirect_dma_start(out=run_rows,
                                        out_offset=bass.IndirectOffsetOnAxis(ap=seam_ids[:, 0:1], axis=0),
                                        in_=seam_max[:, :], in_offset=None).then_inc(ph.seam_stored, 16)
                pool.wait_ge(ph.seam_stored, 16)

            def gather_nodes(ph, freed, per_group):
                def step(it):
                    for b in range(NR):
                        pool.wait_ge(ph.ids_made, NR * it + b + 1)
                        wait_slot(pool, freed, per_group * (NR * (it - 1) + b + 1))
                        apart(pool)
                        for j in range(GT):
                            pool.indirect_dma_start(
                                out=node_in[:, b, j * D:(j + 1) * D], out_offset=None, in_=run_rows,
                                in_offset=bass.IndirectOffsetOnAxis(ap=end_ids[:, b, j:j + 1], axis=0),
                            ).then_inc(ph.gathered[b], 16)

                step(0)
                with pool.Fori(1, NSTEPS) as it:
                    step(it)

            gather_edges(edges[0], msg_table[0], norm.stored)
            mend_seams(edges[0])
            gather_nodes(mid, mid.turned, NT)
            gather_edges(edges[1], msg_table[1], mid.stored)
            mend_seams(edges[1])
            gather_nodes(fin, fin.ready, 1)

        @block.tensor
        def _(pe):
            def turn_group(ph, it, b):
                q = NR * it + b
                pe.wait_ge(ph.ready, q + 1)
                if ph is norm:
                    pe.wait_ge(pool_normed, q + 1)
                wait_slot(pe, ph.copied, NT * (q - 1))
                j = 0
                for n, tiles in enumerate(TP_BANKS):
                    for s in range(tiles):
                        tr = pe.transpose(turn[b % 2][n][0:D, s * NP:(s + 1) * NP],
                                          node_in[0:NP, b, j * D:(j + 1) * D], ident[0:NP, 0:NP])
                        j += 1
                    tr.then_inc(ph.turned, 1)

            def msg_group(ph, layer, it, b):
                q = NR * it + b
                wait_slot(pe, ph.msg_made, q - 1)
                for j in range(GT):
                    if j in COPIES_AT:
                        pe.wait_ge(ph.copied, NT * q + COPIES_AT.index(j) + 1)
                    mm = pe.matmul(bank[b % 2][0:NP, j * D:(j + 1) * D], node_t[:, b, j * NP:(j + 1) * NP],
                                   w_msgs[layer][:, :], start=True, stop=True)
                mm.then_inc(ph.product, 1)

            def root_group(ph, layer, it, b):
                q = NR * it + b
                pe.wait_ge(ph.loaded[b], 16 * (it + 1))
                wait_slot(pe, ph.summed, q - 1)
                to = bank[2 + b % 2]
                for j in range(GT):
                    mm = pe.matmul(to[0:NP, j * D:(j + 1) * D], root_t[:, b, j * NP:(j + 1) * NP],
                                   w_roots[layer][:, :], start=True, stop=True)
                mm.then_inc(ph.root_ready, 1)

            def node_pass(each):
                for b in range(NR):
                    each(0, b)
                with pe.Fori(1, NSTEPS - 1) as it:
                    for b in range(NR):
                        each(it, b)
                for b in range(NR):
                    each(NSTEPS - 1, b)

            def norm_group(it, b):
                msg_group(norm, 0, it, b)
                ahead = it + (b + 2) // NR
                if not isinstance(ahead, int) or ahead < NSTEPS:
                    turn_group(norm, ahead, (b + 2) % NR)

            def mid_group(it, b):
                turn_group(mid, it, b)
                ahead = it + (b + 2) // NR
                if not isinstance(ahead, int) or ahead < NSTEPS:
                    root_group(mid, 0, ahead, (b + 2) % NR)
                msg_group(mid, 1, it, b)

            def fin_pass():
                for b in range(NR):
                    root_group(fin, 1, 0, b)
                with pe.Fori(1, NSTEPS) as it:
                    for b in range(NR):
                        root_group(fin, 1, it, b)

            def histogram(k):
                pe.wait_ge(hot_made, k + 1)
                wait_slot(pe, hist_added, k)
                for t in range(T):
                    mm = pe.matmul(spare_bank[0:NP, 0:NODES], hot_p[:, t, :], hot_j[:, t, :],
                                   start=(t == 0), stop=(t == T - 1))
                mm.then_inc(hist_done, 1)

            def edge_pass(ph, layer):
                def step(i, last=False):
                    for c in range(RING):
                        k = RING * i + c
                        pe.wait_ge(ph.attr_loaded[c], 16 * (i + 1))
                        wait_slot(pe, ph.copied, 3 * k)
                        for g, (t, n) in enumerate(QUADS):
                            into = turn_a if g < 4 else turn_b
                            tr = pe.transpose(into[0:n * DE, (g % 4) * P:(g % 4 + 1) * P],
                                              attr[:, c, t * DE:(t + n) * DE], ident[:, :])
                            if g in (3, NQ - 1):
                                tr.then_inc(ph.turned, 1)
                        if layer == 0 and not (last and c == RING - 1):
                            histogram(k)
                        pe.wait_ge(ph.copied, 3 * (k + 1))
                        one_by_one = last and c == RING - 1
                        if not one_by_one:
                            pe.wait_ge(ph.gathered[c], 16 * T * (i + 1))
                        for g, (t, n) in enumerate(QUADS):
                            if one_by_one and layer == 0 and g == HISTOGRAM_LAST:
                                histogram(k)
                            if one_by_one:
                                pe.wait_ge(ph.last_gathered[g], 16 * n)
                            to = bank[BANK_OF[g]][:, 0:n * D]
                            wait_slot(pe, ph.columns, T * k + freed_columns(g))
                            pe.matmul(to, attr_t[0:n * DE, c, g * P:(g + 1) * P], w_blocks[layer][0:n * DE, 0:n * D],
                                      start=True, stop=False)
                            mm = pe.matmul(to, ident[:, :], rows[:, c, t * D:(t + n) * D], start=False, stop=True)
                            mm.then_inc(ph.msg_ready, 1)

                step(0)
                with pe.Fori(1, STEPS - 1) as i:
                    step(i)
                step(STEPS - 1, last=True)

            def turn_seams(ph):
                pe.wait_ge(ph.columns, EPP)
                pe.transpose(turn_a[0:D, 0:P], run[:, RING - 1, (T - 1) * D:T * D], ident[:, :]
                             ).then_inc(ph.last_turned, 1)
                pe.wait_ge(ph.carried, 1)
                pe.transpose(turn_b[:, 0:D], carry[:, 0:P], ident[0:D, 0:D]).then_inc(ph.carry_turned, 1)

            pe.wait_ge(iotas, 6)
            pe.wait_ge(w_loaded, 16)
            turn_group(norm, 0, 0)
            turn_group(norm, 0, 1)
            node_pass(norm_group)
            pe.wait_ge(others_loaded, 16 * 13)
            pe.wait_ge(norm.msg_made, NG)
            pe.wait_ge(consts_made, 1)
            pe.transpose(turn_a[0:D, 0:P], seam_pen[:, :], ident[:, :]).then_inc(seam_turned, 1)
            pe.wait_ge(seam_turned, 1)
            pe.wait_ge(consts_made, 2)
            edge_pass(edges[0], 0)
            pe.wait_ge(ends_counted, 1)
            pe.matmul(spare_bank[0:NP, 0:1], before[0:NP, 0:NP], hist_sum[:, :], start=True, stop=True
                      ).then_inc(ends_counted, 1)
            turn_seams(edges[0])
            pe.wait_ge(ones_made, 1)
            root_group(mid, 0, 0, 0)
            root_group(mid, 0, 0, 1)
            node_pass(mid_group)
            pe.wait_ge(mid.msg_made, NG)
            edge_pass(edges[1], 1)
            turn_seams(edges[1])
            fin_pass()

        @block.scalar
        def _(act):
            act.dma_start(w_msgs[0][:, :], w_msg[0]).then_inc(w_loaded, 16)
            act.wait_ge(eps_made, 1)
            act.activation(root_of_eps[:, :], eps[:, :], ACT.Sqrt)

            def edge_setup():
                act.dma_start(dst_i, dst_rows).then_inc(dst_loaded, 16)
                act.wait_ge(zeros_made, 2)
                with nc.allow_non_contiguous_dma(reason="one column, once"):
                    act.dma_start(edge_ids[:, 0:1], dst_rows[:, 0:1]).then_inc(dst_loaded, 16)
                    act.dma_start(edge_ids[:, 1:2], dst_rows[:, EPP - 1:EPP]).then_inc(dst_loaded, 16)
                    act.dma_start(edge_ids[1:P, 2:3], dst_rows[0:P - 1, EPP - 1:EPP]).then_inc(dst_loaded, 16)
                    act.dma_start(edge_ids[0:P - 1, 3:4], dst_rows[1:P, 0:1]).then_inc(dst_loaded, 16)
                for z in range(2):
                    act.dma_start(run_rows[E + z * P:E + (z + 1) * P, :], seam_max[:, :]).then_inc(zero_stored, 16)
                act.wait_ge(blocks_zero, 2)
                for l in range(2):
                    for g in range(4):
                        act.dma_start(w_blocks[l][g * DE:(g + 1) * DE, g * D:(g + 1) * D], w_edge[l]
                                      ).then_inc(others_loaded, 16)
                act.dma_start(w_msgs[1][:, :], w_msg[1]).then_inc(others_loaded, 16)
                for l in range(2):
                    act.dma_start(w_roots[l][0:D, :], w_root[l]).then_inc(others_loaded, 16)
                    act.dma_start(w_roots[l][D:D + 1, :], bias[l].unsqueeze(0)).then_inc(others_loaded, 16)

            def deviation(it, b):
                act.wait_ge(var_ready, NR * it + b + 1)
                wait_slot(act, rstd_made, NR * it + b - 1)
                act.activation(std[:, b % 2, :], moments[:, b % 2, :, 1], ACT.Sqrt, bias=eps[0:NP, :]
                               ).then_inc(std_ready, 1)

            def turned_out(ph, it, b):
                wait_slot(act, ph.stored[b], 32 * it)
                at = 0
                for n, tiles in enumerate(TP_BANKS):
                    act.wait_ge(ph.turned, NT * (NR * it + b) + n + 1)
                    act.activation(node_t[:, b, at * NP:(at + tiles) * NP], turn[b % 2][n][0:D, 0:tiles * NP],
                                   ACT.Relu if ph is norm else ACT.Copy).then_inc(ph.copied, 1)
                    at += tiles

            def msg_rows_out(ph, it, b):
                act.wait_ge(ph.product, NR * it + b + 1)
                wait_slot(act, ph.stored[b], 32 * it)
                act.copy(msg_out[:, b, :], bank[b % 2][0:NP, 0:GT * D]).then_inc(ph.msg_made, 1)

            def norm_pass():
                def group(it, b):
                    soon, later = ((it + (b + n) // NR, (b + n) % NR) for n in (1, AHEAD))
                    if not isinstance(soon[0], int) or soon[0] < NSTEPS:
                        turned_out(norm, *soon)
                    if not isinstance(later[0], int) or later[0] < NSTEPS:
                        deviation(*later)
                    msg_rows_out(norm, it, b)
                    store_msg_rows(act, norm, 0, it, b)

                for b in range(AHEAD):
                    deviation(0, b)
                turned_out(norm, 0, 0)
                for b in range(NR):
                    group(0, b)
                with act.Fori(1, NSTEPS - 1) as it:
                    for b in range(NR):
                        group(it, b)
                for b in range(NR):
                    group(NSTEPS - 1, b)

            def mid_pass():
                def step(it):
                    for b in range(NR):
                        turned_out(mid, it, b)
                        store_turned(act, mid, 1, it, b)
                        msg_rows_out(mid, it, b)
                        store_msg_rows(act, mid, 1, it, b)

                step(0)
                with act.Fori(1, NSTEPS) as it:
                    step(it)

            def fin_pass():
                outs = by_group(out)

                def step(it):
                    for b in range(NR):
                        q = NR * it + b
                        act.wait_ge(fin.ready, q + 1)
                        act.dma_start(outs[:, q, :], msg_out[:, b, :]).then_inc(fin.stored[b], 16)

                step(0)
                with act.Fori(1, NSTEPS) as it:
                    step(it)

            def edge_pass(ph):
                def step(i):
                    for c in range(RING):
                        k = RING * i + c
                        wait_slot(act, ph.columns, T * (k - RING + 1))
                        act.copy(pen[:, c, :], penalty[:, bass.ds(T * k, T)]).then_inc(ph.pen_ready, 1)
                        wait_slot(act, ph.msg_ready, NQ * (k - RING + 1))
                        act.wait_ge(ph.turned, 2 * k + 1)
                        act.copy(attr_t[:, c, 0:4 * P], turn_a[:, 0:4 * P]).then_inc(ph.copied, 1)
                        act.wait_ge(ph.turned, 2 * k + 2)
                        act.copy(attr_t[:, c, 4 * P:(NQ - 1) * P], turn_b[:, 0:(NQ - 5) * P]).then_inc(ph.copied, 1)
                        act.copy(attr_t[0:DE, c, (NQ - 1) * P:NQ * P], turn_b[0:DE, (NQ - 5) * P:(NQ - 4) * P]
                                 ).then_inc(ph.copied, 1)

                step(0)
                with act.Fori(1, STEPS) as i:
                    step(i)

            norm_pass()
            for b in range(NR):
                act.wait_ge(norm.stored[b], 32 * NSTEPS)
            edge_setup()
            act.wait_ge(consts_made, 1)
            edge_pass(edges[0])
            mid_pass()
            edge_pass(edges[1])
            fin_pass()

        @block.vector
        def _(dve):
            done = [0]

            def own(ins):
                ins.then_inc(vec, 1)
                done[0] += 1
                dve.wait_ge(vec, done[0])

            dve.memset(eps[:, :], EPS).then_inc(eps_made, 1)
            dve.memset(seam_max[:, :], 0.0).then_inc(zeros_made, 1)
            dve.memset(edge_ids[:, :], -1).then_inc(zeros_made, 1)
            for l in range(2):
                dve.memset(w_blocks[l][:, :], 0.0).then_inc(blocks_zero, 1)
            

            def stats_of(it, b):
                q = NR * it + b
                dve.wait_ge(x_loaded[b], 32 * (it + 1))
                wait_slot(dve, var_ready, q - 1)
                for j in range(GT):
                    ins = dve.bn_stats(stats[:, b % 2, j, :], x_in[:, b, j * D:(j + 1) * D])
                ins.then_inc(bn_made, 1)

            def moments_of(it, b):
                q = NR * it + b
                dve.wait_ge(bn_made, q + 1)
                wait_slot(dve, norm.ready, q - 1)
                wait_slot(dve, pool_normed, q - 1)
                apart(dve)
                for j in range(GT):
                    ins = dve.bn_aggr(moments[:, b % 2, j, :], stats[:, b % 2, j, :])
                ins.then_inc(var_ready, 1)

            def inverted(it, b):
                q = NR * it + b
                dve.wait_ge(std_ready, q + 1)
                wait_slot(dve, norm.ready, q - 1)
                wait_slot(dve, pool_normed, q - 1)
                dve.reciprocal(rstd[:, b % 2, :], std[:, b % 2, :]).then_inc(rstd_made, 1)

            def normed(it, b):
                q = NR * it + b
                dve.wait_ge(rstd_made, q + 1)
                wait_slot(dve, norm.turned, NT * (q - NR + 1))
                for j in range(GT - POOL_TILES):
                    ins = dve.tensor_scalar(node_in[0:NP, b, j * D:(j + 1) * D], x_in[:, b, j * D:(j + 1) * D],
                                            moments[:, b % 2, j, 0:1], rstd[:, b % 2, j:j + 1],
                                            ALU.subtract, ALU.mult)
                ins.then_inc(norm.ready, 1)

            def norm_pass():
                def group(it, b):
                    ahead = (it, b + 1) if b + 1 < NR else (it + 1, 0)
                    inverted(it, b)
                    stats_of(*ahead)
                    normed(it, b)
                    moments_of(*ahead)

                stats_of(0, 0)
                moments_of(0, 0)
                for b in range(NR):
                    group(0, b)
                with dve.Fori(1, NSTEPS - 1) as it:
                    for b in range(NR):
                        group(it, b)
                for b in range(NR - 1):
                    group(NSTEPS - 1, b)
                inverted(NSTEPS - 1, NR - 1)
                normed(NSTEPS - 1, NR - 1)

            def make_ids(ph, it, b):
                wait_slot(dve, ph.gathered[b], 16 * GT * it)
                dve.tensor_scalar(end_ids[0:NP, b, :], ends[:, bass.ds(GT * (NR * it + b), GT)], float(ZERO), None,
                                  ALU.add).then_inc(ph.ids_made, 1)

            def activated(ph, it, b):
                q = NR * it + b
                dve.wait_ge(ph.gathered[b], 16 * GT * (it + 1))
                dve.wait_ge(ph.root_ready, q + 1)
                dve.tensor_tensor(node_in[0:NP, b, :], node_in[0:NP, b, :], bank[2 + b % 2][0:NP, 0:GT * D], ALU.add
                                  ).then_inc(ph.summed, 1)
                dve.wait_ge(ph.summed, q + 1)
                dve.scalar_tensor_tensor(out=node_in[0:NP, b, :], in0=node_in[0:NP, b, :], scalar=SLOPE,
                                         in1=node_in[0:NP, b, :], op0=ALU.mult, op1=ALU.max
                                         ).then_inc(mid.ready if ph is mid else activated_made, 1)

            def mid_pass():
                def step(it, last=False):
                    for b in range(NR):
                        activated(mid, it, b)
                        if not last:
                            make_ids(mid, it + 1, b)

                step(0)
                with dve.Fori(1, NSTEPS - 1) as it:
                    step(it)
                step(NSTEPS - 1, last=True)

            def fin_pass():
                def step(it, last=False):
                    for b in range(NR):
                        activated(fin, it, b)
                        dve.wait_ge(activated_made, NR * it + b + 1)
                        dve.wait_ge(x_loaded[b], 32 * (NSTEPS + it + 1))
                        dve.tensor_tensor(msg_out[:, b, :], msg_out[:, b, :], node_in[0:NP, b, :], ALU.add
                                          ).then_inc(fin.ready, 1)
                        if not last:
                            make_ids(fin, it + 1, b)

                step(0)
                with dve.Fori(1, NSTEPS - 1) as it:
                    step(it)
                step(NSTEPS - 1, last=True)

            def prepare_edges():
                dve.memset(root_t[D:D + 1, :, :], 1.0).then_inc(ones_made, 1)
                dve.memset(end_ids[:, :, :], ZERO)
                dve.wait_ge(iotas, 6)
                dve.wait_ge(norm.copied, NT * NG)
                dve.tensor_copy(iota_bank[:, 0:P], iota_i[:, :])
                dve.wait_ge(dst_loaded, 16 * 5)
                dve.memset(penalty[:, 0:1], 0.0)
                dve.tensor_copy(edge_f[:, :], edge_ids[:, :])
                own(dve.tensor_copy(dst_f, dst_i))
                dve.tensor_tensor(penalty[:, 1:EPP], dst_f[:, 1:EPP], dst_f[:, 0:EPP - 1], ALU.not_equal)
                own(dve.tensor_scalar(tmp_f, dst_f, edge_f[:, 0:1], None, ALU.is_equal))
                dve.tensor_scalar(penalty[:, 1:EPP], penalty[:, 1:EPP], LOW, None, ALU.mult)
                own(dve.tensor_reduce(seam[:, 0:1], tmp_f, AX.X, ALU.add))
                own(dve.tensor_scalar(tmp_f, dst_f, -(NODES - 1) / 2, 1.0 / NODES, ALU.add, ALU.mult))
                own(dve.tensor_scalar(tmp_f, tmp_f, 1.5 * 2 ** 23, -1.5 * 2 ** 23, ALU.add, ALU.add))
                dve.tensor_copy(node_p[:, :], tmp_f)
                own(dve.scalar_tensor_tensor(out=node_j[:, :], in0=tmp_f, scalar=-float(NODES), in1=dst_f,
                                             op0=ALU.mult, op1=ALU.add))
                first, last, prev, nxt = (edge_f[:, n:n + 1] for n in range(4))
                length, open_, ends_here, at = (seam[:, n:n + 1] for n in range(4))
                differs, spare, shift, part = (seam[:, n:n + 1] for n in range(4, 8))
                dve.tensor_copy(part, part_i[:, :])
                dve.tensor_tensor(open_, prev, first, ALU.is_equal)
                dve.tensor_tensor(ends_here, last, first, ALU.not_equal)
                own(dve.tensor_tensor(differs, nxt, first, ALU.not_equal))
                dve.tensor_scalar(spare, part, float(SPARE), None, ALU.add)
                own(dve.tensor_tensor(ends_here, ends_here, differs, ALU.max))
                own(dve.tensor_tensor(open_, open_, ends_here, ALU.mult))
                own(dve.scalar_tensor_tensor(out=shift, in0=part, scalar=float(EPP - 1), in1=length,
                                             op0=ALU.mult, op1=ALU.add))
                own(dve.tensor_scalar(shift, shift, -1.0 - SPARE, None, ALU.add))
                own(dve.tensor_tensor(at, shift, open_, ALU.mult))
                own(dve.tensor_tensor(at, at, spare, ALU.add))
                dve.tensor_copy(seam_ids[:, :], at)
                own(dve.tensor_tensor(differs, last, prev, ALU.not_equal))
                own(dve.tensor_scalar(differs, differs, LOW, None, ALU.mult))
                dve.tensor_copy(seam_pen[:, :], differs.to_broadcast([P, D])).then_inc(consts_made, 1)
                dve.memset(hist[:, :], 0.0)
                dve.memset(carry[:, 0:1], LOW)
                dve.wait_ge(seam_turned, 1)
                dve.tensor_copy(seam_pen_t[:, :], turn_a[0:D, 0:P]).then_inc(consts_made, 1)

            def edge_pass(ph, layer):
                if layer == 0:
                    for b in range(NR):
                        dve.wait_ge(norm.stored[b], 32 * NSTEPS)
                own(dve.memset(run[:, RING - 1, (T - 1) * D:T * D], LOW))

                def one_hots(k):
                    wait_slot(dve, hist_done, k)
                    dve.tensor_tensor(
                        hot_p, iota_bank[:, 0:NP].unsqueeze(1).to_broadcast([P, T, NP]),
                        node_p[:, bass.ds(T * k, T)].unsqueeze(2).to_broadcast([P, T, NP]), ALU.is_equal)
                    dve.tensor_tensor(
                        hot_j, iota_bank[:, 0:NODES].unsqueeze(1).to_broadcast([P, T, NODES]),
                        node_j[:, bass.ds(T * k, T)].unsqueeze(2).to_broadcast([P, T, NODES]), ALU.is_equal
                    ).then_inc(hot_made, 1)

                def step(i, last=False):
                    for c in range(RING):
                        k = RING * i + c
                        hots_at = HOTS_LAST if last and c == RING - 1 else 0
                        dve.wait_ge(ph.pen_ready, k + 1)
                        wait_slot(dve, ph.stored[c], 16 * i)
                        for t in range(T):
                            g, s = t // 4, t % 4
                            if layer == 0 and t == 4 * hots_at:
                                one_hots(k)
                            if s == 0:
                                dve.wait_ge(ph.msg_ready, NQ * k + g + 1)
                            wait_slot(dve, ph.columns, T * k + t)
                            was = run[:, c, (t - 1) * D:t * D] if t else run[:, (c - 1) % RING, (T - 1) * D:T * D]
                            dve.scalar_tensor_tensor(
                                out=run[:, c, t * D:(t + 1) * D], in0=was, scalar=pen[:, c, t:t + 1],
                                in1=bank[BANK_OF[g]][:, s * D:(s + 1) * D], op0=ALU.add, op1=ALU.max
                            ).then_inc(ph.columns, 1)
                        if layer == 0:
                            dve.wait_ge(hist_done, k + 1)
                            dve.tensor_tensor(hist[:, :], hist[:, :], spare_bank[0:NP, 0:NODES], ALU.add
                                              ).then_inc(hist_added, 1)

                step(0)
                with dve.Fori(1, STEPS - 1) as i:
                    step(i)
                step(STEPS - 1, last=True)

            def mend_seams(ph):
                dve.wait_ge(ph.last_turned, 1)
                dve.tensor_tensor_scan(carry[:, 1:1 + P], seam_pen_t[:, :], turn_a[0:D, 0:P], LOW,
                                       ALU.add, ALU.max).then_inc(ph.carried, 1)
                dve.wait_ge(ph.carry_turned, 1)
                dve.wait_ge(ph.seam_gathered, 16)
                dve.tensor_tensor(seam_max[:, :], seam_rows[:, :], turn_b[:, 0:D], ALU.max).then_inc(ph.seam_maxed, 1)

            def count_ends():
                dve.wait_ge(hist_added, STEPS * RING)
                dve.tensor_reduce(hist_sum[:, :], hist[:, :], AX.X, ALU.add).then_inc(ends_counted, 1)
                dve.memset(some[:, :], 1.0)
                dve.wait_ge(ends_counted, 2)
                own(dve.tensor_copy(hist_before[:, :], spare_bank[0:NP, 0:1]))
                own(dve.tensor_tensor_scan(ends[:, :], some[:, :], hist[:, :], hist_before[:, 0:1],
                                           ALU.mult, ALU.add))
                dve.tensor_scalar(ends[:, :], ends[:, :], -1.0 - ZERO, None, ALU.add)
                own(dve.tensor_scalar(some[:, :], hist[:, :], 1.0, None, ALU.min))
                own(dve.tensor_tensor(ends[:, :], ends[:, :], some[:, :], ALU.mult))

            norm_pass()
            prepare_edges()
            edge_pass(edges[0], 0)
            count_ends()
            for b in range(NR):
                make_ids(mid, 0, b)
            mend_seams(edges[0])
            mid_pass()
            edge_pass(edges[1], 1)
            for b in range(NR):
                make_ids(fin, 0, b)
            mend_seams(edges[1])
            fin_pass()


INPUTS = ["x", "src", "dst", "edge_attr_32", "L0_gnn_W1_msg", "L0_gnn_W1_edge", "L0_gnn_W1_root", "L0_gnn_b1",
          "L0_gnn_W2_msg", "L0_gnn_W2_edge", "L0_gnn_W2_root", "L0_gnn_b2"]


def kernel(**inputs):
    import concourse.bacc as bacc
    from concourse.bass_utils import run_bass_kernel_spmd

    nc = bacc.Bacc("TRN2", target_bir_lowering=False, num_devices=1)
    arrays, aps = {}, {}
    for name in INPUTS:
        a = np.ascontiguousarray(inputs[name])
        arrays[f"in_{name}"] = a
        aps[name] = nc.dram_tensor(f"in_{name}", a.shape, mybir.dt.from_np(a.dtype), kind="ExternalInput").ap()
    out = nc.dram_tensor("out", (N, D), F32, kind="ExternalOutput").ap()
    layer = lambda what: [aps[f"L0_gnn_{what.format(n)}"] for n in (1, 2)]
    build(nc, aps["x"], aps["src"], aps["dst"], aps["edge_attr_32"],
          layer("W{}_msg"), layer("W{}_edge"), layer("W{}_root"), layer("b{}"), out)
    r = run_bass_kernel_spmd(nc, [arrays], core_ids=[0])
    return r.results[0]["out"]
```
